# Optimizing a Trainium2 kernel written in Bass

```python
import numpy as np
import jax
import jax.numpy as jnp

def _softmax(x, axis=-1):
    return jax.nn.softmax(x, axis=axis)

def _gelu(x):
    return jax.nn.gelu(x, approximate=True)

def _silu(x):
    return jax.nn.silu(x)

def _sigmoid(x):
    return jax.nn.sigmoid(x)

def _layernorm(x, axis=-1, eps=1e-05):
    m = jnp.mean(x, axis=axis, keepdims=True)
    v = jnp.var(x, axis=axis, keepdims=True)
    return (x - m) / jnp.sqrt(v + eps)

def _scatter_add(tgt, idx, src, axis=0):
    return tgt.at[idx].add(src)

def _segment_sum(src, seg, n):
    return jax.ops.segment_sum(src, seg, n)
kernel_name = 'mk_dlrm_tower_d1_rec_r8_202139'

def setup_inputs(seed: int=0):
    np.random.seed(seed)
    _w = jnp.asarray

    def _rec_inputs():
        import jax
        import jax.numpy as jnp
        _tk = jax.random.key(seed)
        ids = jnp.stack([jax.random.randint(jax.random.fold_in(_tk, 200 + f), (512,), 0, v, jnp.int32) for f, v in enumerate([1250, 125000, 1000, 1000, 1250, 1000, 1250, 12500, 1000, 1250, 1250, 12500, 12500, 1000, 1000, 12500, 1250, 1000, 1250, 1000, 12500, 1250, 1250, 1250, 12500, 1250])], axis=1)
        tbl_0 = 0.05 * jax.random.normal(jax.random.fold_in(_tk, 500 + 0), (1250, 128), jnp.float32)
        tbl_1 = 0.05 * jax.random.normal(jax.random.fold_in(_tk, 500 + 1), (125000, 128), jnp.float32)
        tbl_2 = 0.05 * jax.random.normal(jax.random.fold_in(_tk, 500 + 2), (1000, 128), jnp.float32)
        tbl_3 = 0.05 * jax.random.normal(jax.random.fold_in(_tk, 500 + 3), (1000, 128), jnp.float32)
        tbl_4 = 0.05 * jax.random.normal(jax.random.fold_in(_tk, 500 + 4), (1250, 128), jnp.float32)
        tbl_5 = 0.05 * jax.random.normal(jax.random.fold_in(_tk, 500 + 5), (1000, 128), jnp.float32)
        tbl_6 = 0.05 * jax.random.normal(jax.random.fold_in(_tk, 500 + 6), (1250, 128), jnp.float32)
        tbl_7 = 0.05 * jax.random.normal(jax.random.fold_in(_tk, 500 + 7), (12500, 128), jnp.float32)
        tbl_8 = 0.05 * jax.random.normal(jax.random.fold_in(_tk, 500 + 8), (1000, 128), jnp.float32)
        tbl_9 = 0.05 * jax.random.normal(jax.random.fold_in(_tk, 500 + 9), (1250, 128), jnp.float32)
        tbl_10 = 0.05 * jax.random.normal(jax.random.fold_in(_tk, 500 + 10), (1250, 128), jnp.float32)
        tbl_11 = 0.05 * jax.random.normal(jax.random.fold_in(_tk, 500 + 11), (12500, 128), jnp.float32)
        tbl_12 = 0.05 * jax.random.normal(jax.random.fold_in(_tk, 500 + 12), (12500, 128), jnp.float32)
        tbl_13 = 0.05 * jax.random.normal(jax.random.fold_in(_tk, 500 + 13), (1000, 128), jnp.float32)
        tbl_14 = 0.05 * jax.random.normal(jax.random.fold_in(_tk, 500 + 14), (1000, 128), jnp.float32)
        tbl_15 = 0.05 * jax.random.normal(jax.random.fold_in(_tk, 500 + 15), (12500, 128), jnp.float32)
        tbl_16 = 0.05 * jax.random.normal(jax.random.fold_in(_tk, 500 + 16), (1250, 128), jnp.float32)
        tbl_17 = 0.05 * jax.random.normal(jax.random.fold_in(_tk, 500 + 17), (1000, 128), jnp.float32)
        tbl_18 = 0.05 * jax.random.normal(jax.random.fold_in(_tk, 500 + 18), (1250, 128), jnp.float32)
        tbl_19 = 0.05 * jax.random.normal(jax.random.fold_in(_tk, 500 + 19), (1000, 128), jnp.float32)
        tbl_20 = 0.05 * jax.random.normal(jax.random.fold_in(_tk, 500 + 20), (12500, 128), jnp.float32)
        tbl_21 = 0.05 * jax.random.normal(jax.random.fold_in(_tk, 500 + 21), (1250, 128), jnp.float32)
        tbl_22 = 0.05 * jax.random.normal(jax.random.fold_in(_tk, 500 + 22), (1250, 128), jnp.float32)
        tbl_23 = 0.05 * jax.random.normal(jax.random.fold_in(_tk, 500 + 23), (1250, 128), jnp.float32)
        tbl_24 = 0.05 * jax.random.normal(jax.random.fold_in(_tk, 500 + 24), (12500, 128), jnp.float32)
        tbl_25 = 0.05 * jax.random.normal(jax.random.fold_in(_tk, 500 + 25), (1250, 128), jnp.float32)
        _rk = jax.random.fold_in(_tk, 7)
        r_dense_x = -0.000514642 + 1.00011 * jax.random.normal(jax.random.fold_in(_rk, 101), (512, 128), jnp.float32)
        W_top1 = 0.0456912 * jax.random.normal(jax.random.fold_in(_tk, 801), (479, 512), jnp.float32)
        W_top2 = 0.0441942 * jax.random.normal(jax.random.fold_in(_tk, 802), (512, 256), jnp.float32)
        W_top3 = 0.0625 * jax.random.normal(jax.random.fold_in(_tk, 803), (256, 1), jnp.float32)
        b_top1 = jnp.zeros((512,), jnp.float32)
        b_top2 = jnp.zeros((256,), jnp.float32)
        return (r_dense_x, ids, tbl_0, tbl_1, tbl_2, tbl_3, tbl_4, tbl_5, tbl_6, tbl_7, tbl_8, tbl_9, tbl_10, tbl_11, tbl_12, tbl_13, tbl_14, tbl_15, tbl_16, tbl_17, tbl_18, tbl_19, tbl_20, tbl_21, tbl_22, tbl_23, tbl_24, tbl_25, W_top1, b_top1, W_top2, b_top2, W_top3)
    r_dense_x, ids, tbl_0, tbl_1, tbl_2, tbl_3, tbl_4, tbl_5, tbl_6, tbl_7, tbl_8, tbl_9, tbl_10, tbl_11, tbl_12, tbl_13, tbl_14, tbl_15, tbl_16, tbl_17, tbl_18, tbl_19, tbl_20, tbl_21, tbl_22, tbl_23, tbl_24, tbl_25, W_top1, b_top1, W_top2, b_top2, W_top3 = _rec_inputs()

    def _L0_rec_setup():
        import jax, jax.numpy as jnp
        import numpy as np
        F = 26
        D = 128
        B = 2048
        _TRIU_I, _TRIU_J = np.triu_indices(F + 1, k=1)
        _TRIU_I = jnp.asarray(_TRIU_I)
        _TRIU_J = jnp.asarray(_TRIU_J)
        key = jax.random.key(seed)
        k1, k2 = jax.random.split(key)
        sparse_x = jax.random.normal(k1, (B, F, D), dtype=jnp.float32)
        dense_x = jax.random.normal(k2, (B, D), dtype=jnp.float32)
        return {'sparse_x': sparse_x, 'dense_x': dense_x}
    _L0_rec_all = _L0_rec_setup()
    _L0_rec_in = {k: v for k, v in _L0_rec_all.items() if k in ()}
    del _L0_rec_all
    return {'r_dense_x': r_dense_x, 'ids': ids, 'tbl_0': tbl_0, 'tbl_1': tbl_1, 'tbl_2': tbl_2, 'tbl_3': tbl_3, 'tbl_4': tbl_4, 'tbl_5': tbl_5, 'tbl_6': tbl_6, 'tbl_7': tbl_7, 'tbl_8': tbl_8, 'tbl_9': tbl_9, 'tbl_10': tbl_10, 'tbl_11': tbl_11, 'tbl_12': tbl_12, 'tbl_13': tbl_13, 'tbl_14': tbl_14, 'tbl_15': tbl_15, 'tbl_16': tbl_16, 'tbl_17': tbl_17, 'tbl_18': tbl_18, 'tbl_19': tbl_19, 'tbl_20': tbl_20, 'tbl_21': tbl_21, 'tbl_22': tbl_22, 'tbl_23': tbl_23, 'tbl_24': tbl_24, 'tbl_25': tbl_25, 'W_top1': W_top1, 'b_top1': b_top1, 'W_top2': W_top2, 'b_top2': b_top2, 'W_top3': W_top3}

def reference(r_dense_x, ids, tbl_0, tbl_1, tbl_2, tbl_3, tbl_4, tbl_5, tbl_6, tbl_7, tbl_8, tbl_9, tbl_10, tbl_11, tbl_12, tbl_13, tbl_14, tbl_15, tbl_16, tbl_17, tbl_18, tbl_19, tbl_20, tbl_21, tbl_22, tbl_23, tbl_24, tbl_25, W_top1, b_top1, W_top2, b_top2, W_top3):
    import jax
    import jax.numpy as jnp

    def _L0_rec_ref(sparse_x, dense_x):
        import jax, jax.numpy as jnp
        import numpy as np
        F = 26
        D = 128
        B = 2048
        _TRIU_I, _TRIU_J = np.triu_indices(F + 1, k=1)
        _TRIU_I = jnp.asarray(_TRIU_I)
        _TRIU_J = jnp.asarray(_TRIU_J)
        combined = jnp.concatenate([sparse_x, dense_x[:, None, :]], axis=1)
        interact = jnp.einsum('bfd,bgd->bfg', combined, combined)
        return interact[:, _TRIU_I, _TRIU_J]
    e = jnp.stack([tbl_0[ids[:, 0]], tbl_1[ids[:, 1]], tbl_2[ids[:, 2]], tbl_3[ids[:, 3]], tbl_4[ids[:, 4]], tbl_5[ids[:, 5]], tbl_6[ids[:, 6]], tbl_7[ids[:, 7]], tbl_8[ids[:, 8]], tbl_9[ids[:, 9]], tbl_10[ids[:, 10]], tbl_11[ids[:, 11]], tbl_12[ids[:, 12]], tbl_13[ids[:, 13]], tbl_14[ids[:, 14]], tbl_15[ids[:, 15]], tbl_16[ids[:, 16]], tbl_17[ids[:, 17]], tbl_18[ids[:, 18]], tbl_19[ids[:, 19]], tbl_20[ids[:, 20]], tbl_21[ids[:, 21]], tbl_22[ids[:, 22]], tbl_23[ids[:, 23]], tbl_24[ids[:, 24]], tbl_25[ids[:, 25]]], axis=1)
    z = _L0_rec_ref(e, r_dense_x)
    z = z.reshape(z.shape[0], -1)
    h = jnp.concatenate([z, r_dense_x], axis=1)
    h = jnp.maximum(h @ W_top1 + b_top1, 0.0)
    h = jnp.maximum(h @ W_top2 + b_top2, 0.0)
    y = h @ W_top3
    return y

_drawn_inputs = setup_inputs


def setup_inputs(seed=0):
    import zlib

    import numpy as np

    out = dict(_drawn_inputs(seed))
    spreads = {'b_top1': (0.0, 0.1), 'b_top2': (0.0, 0.1)}
    factors = {}
    for name, (base, spread) in spreads.items():
        noise = np.random.default_rng([zlib.crc32(name.encode()), seed]).standard_normal(out[name].shape)
        drawn = base * np.exp(spread * noise) if base else spread * noise
        out[name] = jnp.asarray(drawn.astype(out[name].dtype))
    for name, factor in factors.items():
        out[name] = (out[name] * factor).astype(out[name].dtype)
    return out
```

```python
import concourse.bass as bass
from concourse import mybir
from contextlib import ExitStack

ALU = mybir.AluOpType
ACT = mybir.ActivationFunctionType
F32 = mybir.dt.float32
I32 = mybir.dt.int32
U32 = mybir.dt.uint32

P = 128
NF = 26
NV = NF + 1
SLOT = 32
SLOTS = P // SLOT
GT = -(-NF // SLOTS)
TG = 4
FG = [range(a, min(a + TG, NF)) for a in range(0, NF, TG)]
NG = len(FG)
QB = 16
BANK = 512


def dlrm_tower(nc, xT, ids, tables, w1, w1x, b1, w2, b2, w3, out):
    B = ids.shape[0]
    D = xT.shape[0]
    N1, N2 = w2.shape
    C1, C2 = N1 // P, N2 // P
    NT = B // P
    PAIRS = NT // 2
    QN = P // SLOTS
    QH = QN // QB
    assert D == P and NT % 2 == 0 and QB * NV <= BANK


    ctx = ExitStack()
    with ctx:
        def sb(name, shape, dt=F32):
            return ctx.enter_context(nc.sbuf_tensor(name, shape, dt))

        def pb(name, shape):
            return ctx.enter_context(nc.psum_tensor(name, shape, F32))

        def sem(name):
            return ctx.enter_context(nc.semaphore(name))

        ident = sb("ident", [P, P])
        w1_sb = sb("w1_sb", [P, GT, N1])
        w1x_sb = sb("w1x_sb", [D, N1])
        w2_sb = sb("w2_sb", [P, C1, N2])
        w3_sb = sb("w3_sb", [P, C2])
        b1_sb = sb("b1_sb", [P, C1])
        b2_sb = sb("b2_sb", [P, C2])
        x_all = sb("x_all", [D, B])
        idx = sb("idx", [P, NT, NF], I32)
        rows = [sb(f"rows{i}", [P, NF, D]) for i in range(2)]
        x_cur = [sb(f"x_cur{i}", [D, P]) for i in range(2)]
        vT = [sb(f"vT{i}", [D, P, SLOT]) for i in range(2)]
        z_sb = sb("z_sb", [P, GT, P])
        h1_sb = sb("h1_sb", [P, C1, P])
        h2_sb = sb("h2_sb", [P, C2, P])
        y_sb = sb("y_sb", [P, NT])

        tr_ps = [pb(f"tr_ps{i}", [P, TG, P]) for i in range(2)]
        z_ps = pb("z_ps", [P, QH, BANK])
        h1_ps = [pb(f"h1_ps{s}", [P, BANK]) for s in range(2)]
        h2_ps = pb("h2_ps", [P, BANK])
        y_ps = pb("y_ps", [P, BANK])

        w_loaded = sem("w_loaded")
        x_loaded = sem("x_loaded")
        ids_loaded = sem("ids_loaded")
        ident_zero = sem("ident_zero")
        ident_made = sem("ident_made")
        z_cleared = sem("z_cleared")
        gathered = [[sem(f"gathered{i}_{k}") for k in range(NG)] for i in range(2)]
        rows_free = [sem(f"rows_free{i}") for i in range(2)]
        transposed = [sem(f"transposed{s}") for s in range(2)]
        tr_free = [sem(f"tr_free{s}") for s in range(2)]
        x_placed = sem("x_placed")
        z_made = sem("z_made")
        z_moved = [sem(f"z_moved{s}") for s in range(2)]
        h1_made = [sem(f"h1_made{s}") for s in range(2)]
        h1_kept = [sem(f"h1_kept{s}") for s in range(2)]
        h2_made = sem("h2_made")
        h2_kept = sem("h2_kept")
        y_made = sem("y_made")
        y_kept = sem("y_kept")
        stored = sem("stored")

        def bank(par, k):
            return (NG * par + k) % 2

        def turn(it, par, k):
            return NG * it + (NG * par + k) // 2

        def groups_done(it, par, s):
            return NG * it + (NG * (par + 1) + (1 - s)) // 2

        block = ctx.enter_context(nc.Block())

        @block.sync
        def _(sp):
            sp.dma_start(idx[:, :, :], ids.rearrange("(p t) f -> p t f", t=NT)).then_inc(ids_loaded, 16)
            sp.dma_start(x_all[:, :], xT).then_inc(x_loaded, 16)
            for dst, src in ((w1_sb, w1), (w1x_sb, w1x), (w2_sb, w2.rearrange("(c p) n -> p c n", p=P)),
                             (w3_sb, w3), (b1_sb, b1), (b2_sb, b2)):
                sp.dma_start(dst[:], src).then_inc(w_loaded, 16)
            sp.wait_ge(y_kept, NT)
            sp.dma_start(out.rearrange("(p t) o -> p (t o)", t=NT), y_sb[:, :]).then_inc(stored, 16)
            sp.wait_ge(stored, 16)

        @block.gpsimd
        def _(pool):
            pool.wait_ge(ident_zero, 1)
            pool.affine_select(out=ident[:, :], in_=ident[:, :], compare_op=ALU.not_equal, fill=1.0,
                               base=0, pattern=[[-1, P]], channel_multiplier=1).then_inc(ident_made, 1)
            pool.wait_ge(ids_loaded, 16)
            for t in range(NT):
                it, par = divmod(t, 2)
                if it:
                    pool.wait_ge(rows_free[par], it)
                for k, group in enumerate(FG):
                    for f in group:
                        pool.indirect_dma_start(
                            rows[par][:, f, :], None, tables[f],
                            bass.IndirectOffsetOnAxis(idx[:, t, f:f + 1].bitcast(U32), 0),
                        ).then_inc(gathered[par][k], 16)

        @block.tensor
        def _(pe):
            pe.wait_ge(ident_made, 1)
            with pe.Fori(0, PAIRS) as it:
                for par in range(2):
                    tile = 2 * it + par
                    for k, group in enumerate(FG):
                        s = bank(par, k)
                        pe.wait_ge(gathered[par][k], 16 * len(group) * (it + 1))
                        pe.wait_ge(tr_free[s], turn(it, par, k) + 1)
                        for i, f in enumerate(group):
                            last = nc.tensor.transpose(tr_ps[s][:, i, :], rows[par][:, f, :], ident[:, :])
                        last.then_inc(transposed[s], 1)
                    for s in range(2):
                        pe.wait_ge(tr_free[s], groups_done(it, par, s) + 1)
                    pe.wait_ge(x_placed, tile + 1)
                    for q in range(QN):
                        for j in range(SLOTS):
                            v = vT[par][:, QN * j + q, 0:NV]
                            c = NV * (q % QB)
                            last = nc.tensor.matmul(z_ps[SLOT * j:SLOT * j + NV, q // QB, c:c + NV], v, v,
                                                    start=True, stop=True)
                        if q == 0:
                            last.then_inc(rows_free[par], 1)
                    last.then_inc(z_made, 1)
                    pe.wait_ge(w_loaded, 16 * 6)
                    for s in range(2):
                        pe.wait_ge(z_moved[s], tile + 1)
                    for c in range(C1):
                        n = slice(P * c, P * c + P)
                        s, i = divmod(c, C1 // 2)
                        acc = h1_ps[s][:, P * i:P * i + P]
                        nc.tensor.matmul(acc, w1x_sb[:, n], x_cur[par][:, :], start=True, stop=False)
                        for g in range(GT):
                            last = nc.tensor.matmul(acc, w1_sb[:, g, n], z_sb[:, g, :],
                                                    start=False, stop=(g == GT - 1))
                        if i == C1 // 2 - 1:
                            last.then_inc(h1_made[s], 1)
                    for s in range(2):
                        pe.wait_ge(h1_kept[s], tile + 1)
                    for m in range(C2):
                        for c in range(C1):
                            last = nc.tensor.matmul(h2_ps[:, P * m:P * m + P], w2_sb[:, c, P * m:P * m + P],
                                                    h1_sb[:, c, :], start=(c == 0), stop=(c == C1 - 1))
                    last.then_inc(h2_made, 1)
                    pe.wait_ge(h2_kept, tile + 1)
                    for m in range(C2):
                        last = nc.tensor.matmul(y_ps[:, 0:1], h2_sb[:, m, :], w3_sb[:, m:m + 1],
                                                start=(m == 0), stop=(m == C2 - 1))
                    last.then_inc(y_made, 1)

        def copy_groups(eng, s, copy, it, par):
            for k, group in enumerate(FG):
                if bank(par, k) == s:
                    eng.wait_ge(transposed[s], turn(it, par, k) + 1)
                    f = group[0]
                    copy(vT[par][:, :, f:f + len(group)].rearrange("d p f -> d f p"),
                         tr_ps[s][:, 0:len(group), :]).then_inc(tr_free[s], 1)

        def move_z(eng, s, copy, it, par):
            eng.wait_ge(z_made, 2 * it + par + 1)
            for j in (2 * s, 2 * s + 1):
                for r in range(SLOTS):
                    n = len(range(1 + r, NV, SLOTS))
                    src = z_ps[SLOT * j:SLOT * j + NV, :, 0:QB * NV]\
                        .rearrange("f h (q g) -> f g h q", g=NV)[:, 1 + r:NV:SLOTS]
                    dst = z_sb[SLOT * r:SLOT * r + NV, 0:n, QN * j:QN * j + QN]\
                        .rearrange("f g (h q) -> f g h q", h=QH)
                    last = copy(dst, src)
            last.then_inc(z_moved[s], 1)

        @block.vector
        def _(dve):
            nc.vector.memset(ident[:, :], 0.0).then_inc(ident_zero, 1)
            nc.vector.memset(z_sb[:, :, :], 0.0).then_inc(z_cleared, 1)
            for s in range(2):
                dve.sem_inc(tr_free[s], 1)
            dve.wait_ge(z_cleared, 1)
            dve.wait_ge(w_loaded, 16 * 6)
            with dve.Fori(0, PAIRS) as it:
                for par in range(2):
                    tile = 2 * it + par
                    copy_groups(dve, 0, nc.vector.tensor_copy, it, par)
                    move_z(dve, 0, nc.vector.tensor_copy, it, par)
                    dve.wait_ge(h1_made[0], tile + 1)
                    for c in range(C1 // 2):
                        last = nc.vector.tensor_scalar(h1_sb[:, c, :], h1_ps[0][:, P * c:P * c + P], b1_sb[:, c:c + 1], 0.0,
                                                       ALU.add, ALU.max)
                    last.then_inc(h1_kept[0], 1)

        @block.scalar
        def _(act):
            def copy(dst, src):
                return nc.scalar.activation(dst, src, ACT.Copy)

            act.wait_ge(x_loaded, 16)
            act.wait_ge(w_loaded, 16 * 6)
            act.wait_ge(z_cleared, 1)
            with act.Fori(0, PAIRS) as it:
                for par in range(2):
                    tile = 2 * it + par
                    xt = x_all[:, :].rearrange("d (p t) -> d t p", t=NT)[:, bass.ds(tile, 1), :]
                    copy(x_cur[par][:, :], xt.rearrange("d a p -> d (a p)"))
                    copy(vT[par][:, :, NF], xt.rearrange("d a p -> d (a p)")).then_inc(x_placed, 1)
                    copy_groups(act, 1, copy, it, par)
                    move_z(act, 1, copy, it, par)
                    act.wait_ge(h1_made[1], tile + 1)
                    for i in range(C1 // 2):
                        c = C1 // 2 + i
                        last = nc.scalar.activation(h1_sb[:, c, :], h1_ps[1][:, P * i:P * i + P], ACT.Relu,
                                                    bias=b1_sb[:, c:c + 1])
                    last.then_inc(h1_kept[1], 1)
                    act.wait_ge(h2_made, tile + 1)
                    for m in range(C2):
                        last = nc.scalar.activation(h2_sb[:, m, :], h2_ps[:, P * m:P * m + P], ACT.Relu,
                                                    bias=b2_sb[:, m:m + 1])
                    last.then_inc(h2_kept, 1)
                    act.wait_ge(y_made, tile + 1)
                    copy(y_sb[:, bass.ds(tile, 1)], y_ps[:, 0:1]).then_inc(y_kept, 1)


def kernel(**inputs):
    import numpy as np
    import concourse.bacc as bacc
    from concourse.bass_utils import run_bass_kernel_spmd

    nc = bacc.Bacc("TRN2", target_bir_lowering=False, num_devices=1)
    arrays = {}

    def dram(name, a):
        arrays[name] = np.ascontiguousarray(a)
        return nc.dram_tensor(name, a.shape, mybir.dt.from_np(a.dtype), kind="ExternalInput").ap()

    x = np.asarray(inputs["r_dense_x"])
    W1 = np.asarray(inputs["W_top1"])
    N1 = W1.shape[1]
    w1 = np.zeros((P, GT, N1), W1.dtype)
    f, g = np.triu_indices(NV, k=1)
    w1[SLOT * ((g - 1) % SLOTS) + f, (g - 1) // SLOTS] = W1[:len(f)]
    args = [dram("xT", x.T), dram("ids", np.asarray(inputs["ids"])),
            [dram(f"tbl_{i}", np.asarray(inputs[f"tbl_{i}"])) for i in range(NF)],
            dram("w1", w1), dram("w1x", W1[len(f):]),
            dram("b1", np.asarray(inputs["b_top1"]).reshape(-1, P).T),
            dram("w2", np.asarray(inputs["W_top2"])),
            dram("b2", np.asarray(inputs["b_top2"]).reshape(-1, P).T),
            dram("w3", np.asarray(inputs["W_top3"]).reshape(-1, P).T)]
    out = nc.dram_tensor("y", (x.shape[0], 1), F32, kind="ExternalOutput").ap()
    dlrm_tower(nc, *args, out)
    return run_bass_kernel_spmd(nc, [arrays], core_ids=[0]).results[0]["y"]
```

```python
import concourse.bass as bass
from concourse import mybir
from contextlib import ExitStack

ALU = mybir.AluOpType
ACT = mybir.ActivationFunctionType
F32 = mybir.dt.float32
F32R = mybir.dt.float32r
I32 = mybir.dt.int32
U32 = mybir.dt.uint32

P = 128
BANK = 512
NF = 26
NV = NF + 1
NZ = NV - 1
SLOT = 32
SLOTS = P // SLOT
GT = -(-NF // SLOTS)
TG = 4
QB = 16
WARM = 23
MAX_PICKED = 8


def feature_order(n_rows):
    picked = sorted(sorted(range(NF), key=lambda f: n_rows[f])[:MAX_PICKED])
    gathered = [f for f in range(NF) if f not in picked]
    return gathered, picked


def dlrm_tower(nc, xT, ids, ids_rows, tables, w1, w1x, b1, w2, b2, w3, out):
    B = ids.shape[0]
    D = xT.shape[0]
    N1, N2 = w2.shape
    C1, C2 = N1 // P, N2 // P
    NT = B // P
    QN = P // SLOTS
    QH = QN // QB
    GF, PF = feature_order([a.shape[0] for a in tables])
    NGF, NPF = len(GF), len(PF)
    GROUPS = [range(a, min(a + TG, NGF)) for a in range(0, NGF, TG)]
    LAST = len(GROUPS) - 1
    AFTER_PICK = {NPF - 1 - len(GROUPS) + k: k for k in range(len(GROUPS))}
    L1_AFTER = {1: (0, 1), LAST - 1: (2,), LAST: (3,)}
    assert C1 == 4
    W_AFTER = NPF - 1
    AHEAD = 3
    ROWS = tables[PF[0]].shape[0]
    R = next(r for r in range(1, ROWS + 1) if ROWS % r == 0 and ROWS // r <= P)
    KP = ROWS // R
    assert D == P and QB * NZ <= BANK and B <= BANK and all(tables[f].shape[0] == ROWS for f in PF)

    ctx = ExitStack()
    with ctx:
        def sb(name, shape, dt=F32):
            return ctx.enter_context(nc.sbuf_tensor(name, shape, dt))

        def pb(name, shape):
            return ctx.enter_context(nc.psum_tensor(name, shape, F32))

        def sem(name):
            return ctx.enter_context(nc.semaphore(name))

        ident = sb("ident", [P, P])
        row_id = sb("row_id", [KP, R], I32)
        minus_row = sb("minus_row", [KP, 1])
        apart = sb("apart", [KP, 2, B])
        idx = sb("idx", [P, NT, NF], I32)
        picks = sb("picks", [KP, NPF, B], I32)
        tbl = sb("tbl", [KP, NPF, R, D])
        tbl_hi = sb("tbl_hi", [KP, 2, R, D], F32R)
        tbl_lo = sb("tbl_lo", [KP, 2, R, D], F32R)
        hot = [sb(f"hot{i}", [KP, R, B], F32R) for i in range(2)]
        px = sb("px", [D, NPF + 1, B])
        w1_sb = sb("w1_sb", [P, GT, N1])
        w1x_sb = sb("w1x_sb", [D, N1])
        w2_sb = sb("w2_sb", [P, C1, N2])
        w3_sb = sb("w3_sb", [P, C2])
        b1_sb = sb("b1_sb", [P, C1])
        b2_sb = sb("b2_sb", [P, C2])
        rows = sb("rows", [P, NGF, D])
        vT = sb("vT", [D, P, NV])
        z_sb = sb("z_sb", [P, GT, P])
        h1_sb = sb("h1_sb", [P, C1, P])
        h2_sb = sb("h2_sb", [P, C2, P])
        y_sb = sb("y_sb", [P, NT])

        tr_ps = [pb(f"tr_ps{i}", [P, TG, P]) for i in range(2)]
        z_ps = pb("z_ps", [P, QH, BANK])
        h1_ps = [pb(f"h1_ps{s}", [P, BANK]) for s in range(2)]
        h2_ps = pb("h2_ps", [P, BANK])
        y_ps = pb("y_ps", [P, BANK])

        ids_loaded = sem("ids_loaded")
        picks_loaded = [sem(f"picks_loaded{i}") for i in range(NPF)]
        tbl_loaded = [sem(f"tbl_loaded{i}") for i in range(NPF)]
        w_loaded = sem("w_loaded")
        x_loaded = sem("x_loaded")
        ident_zero = sem("ident_zero")
        ident_made = sem("ident_made")
        row_id_made = sem("row_id_made")
        z_cleared = sem("z_cleared")
        hi_made = sem("hi_made")
        lo_made = sem("lo_made")
        minus_row_made = sem("minus_row_made")
        hot_made = sem("hot_made")
        apart_made = sem("apart_made")
        last_hot_made = sem("last_hot_made")
        picked = sem("picked")
        pick_kept = sem("pick_kept")
        gathered = [sem(f"gathered{k}") for k in range(len(GROUPS))]
        transposed = [sem(f"transposed{k}") for k in range(len(GROUPS))]
        vt_copied = [sem(f"vt_copied{k}") for k in range(len(GROUPS))]
        px_placed = sem("px_placed")
        z_made = sem("z_made")
        z_moved = [sem(f"z_moved{s}") for s in range(2)]
        h1_made = [sem(f"h1_made{s}") for s in range(2)]
        h1_kept = [sem(f"h1_kept{s}") for s in range(2)]
        h2_made = sem("h2_made")
        h2_kept = sem("h2_kept")
        y_made = sem("y_made")
        y_kept = sem("y_kept")
        stored = sem("stored")
        N_W = 6

        block = ctx.enter_context(nc.Block())

        @block.sync
        def _(sp):
            sp.dma_start(idx[:, :, :], ids.rearrange("(p t) f -> p t f", t=NT)).then_inc(ids_loaded, 16)

            for i, f in enumerate(PF):
                if i >= AHEAD:
                    sp.wait_ge(hi_made, i - AHEAD + 1)
                sp.dma_start(picks[:, i, :], ids_rows[i:i + 1, :].broadcast_to([KP, B])).then_inc(picks_loaded[i], 16)
                sp.dma_start(tbl[:, i, :, :], tables[f].rearrange("(p r) d -> p r d", r=R)).then_inc(tbl_loaded[i], 16)
            sp.dma_start(px[:, NPF, :], xT).then_inc(x_loaded, 16)
            sp.wait_ge(hi_made, W_AFTER)
            for dst, src in ((b1_sb, b1), (b2_sb, b2), (w3_sb, w3), (w1x_sb, w1x), (w1_sb, w1),
                             (w2_sb, w2.rearrange("(c p) n -> p c n", p=P))):
                sp.dma_start(dst[:], src).then_inc(w_loaded, 16)
            sp.wait_ge(y_kept, NT)
            sp.dma_start(out.rearrange("(p t) o -> p (t o)", t=NT), y_sb[:, :]).then_inc(stored, 16)
            sp.wait_ge(stored, 16)

        @block.gpsimd
        def _(pool):
            pool.iota(row_id[:, :], [[1, R]], base=0, channel_multiplier=R).then_inc(row_id_made, 1)
            pool.wait_ge(ident_zero, 1)
            pool.affine_select(out=ident[:, :], in_=ident[:, :], compare_op=ALU.not_equal, fill=1.0,
                               base=0, pattern=[[-1, P]], channel_multiplier=1).then_inc(ident_made, 1)
            pool.wait_ge(ids_loaded, 16)
            for t in range(NT):
                for k, group in enumerate(GROUPS):
                    if t:
                        pool.wait_ge(transposed[k], t)
                    for u in group:
                        pool.indirect_dma_start(
                            rows[:, u, :], None, tables[GF[u]],
                            bass.IndirectOffsetOnAxis(idx[:, t, GF[u]:GF[u] + 1].bitcast(U32), 0),
                        ).then_inc(gathered[k], 16)

        @block.tensor
        def _(pe):
            def pick(i):
                acc = h1_ps[i % 2]
                if i >= 2:
                    pe.wait_ge(pick_kept, i - 1)
                pe.wait_ge(hi_made, i + 1)
                for r in range(R):
                    if r < R - 1:
                        pe.wait_ge(hot_made, (R - 1) * i + r + 1)
                    else:
                        pe.wait_ge(last_hot_made, i + 1)
                    nc.tensor.matmul(acc[:, 0:B], tbl_hi[:, i % 2, r, :], hot[i % 2][:, r, :], start=(r == 0), stop=False)
                pe.wait_ge(lo_made, i + 1)
                for r in range(R):
                    last = nc.tensor.matmul(acc[:, 0:B], tbl_lo[:, i % 2, r, :], hot[i % 2][:, r, :],
                                            start=False, stop=(r == R - 1))
                last.then_inc(picked, 1)

            def transpose(t, k, first):
                pe.wait_ge(gathered[k], 16 * len(GROUPS[k]) * (t + 1))
                if k >= 2:
                    pe.wait_ge(vt_copied[k - 2], t + 1)
                elif not first:
                    pe.wait_ge(vt_copied[max(j for j in range(len(GROUPS)) if j % 2 == k)], t)
                for i, u in enumerate(GROUPS[k]):
                    last = nc.tensor.transpose(tr_ps[k % 2][:, i, :], rows[:, u, :], ident[:, :])
                last.then_inc(transposed[k], 1)

            def interact(t):
                for k in range(len(GROUPS)):
                    pe.wait_ge(vt_copied[k], t + 1)
                pe.wait_ge(px_placed, t + 1)
                for q in range(QN):
                    for j in range(SLOTS):
                        v = vT[:, QN * j + q, :]
                        c = NZ * (q % QB)
                        last = nc.tensor.matmul(z_ps[SLOT * j:SLOT * j + NZ, q // QB, c:c + NZ],
                                                v[:, 0:NZ], v[:, 1:NV], start=True, stop=True)
                last.then_inc(z_made, 1)

            def layer1(t, chunks):
                for c in chunks:
                    n = slice(P * c, P * c + P)
                    s, i = divmod(c, C1 // 2)
                    acc = h1_ps[s][:, P * i:P * i + P]
                    nc.tensor.matmul(acc, w1x_sb[:, n], px[:, NPF, bass.ds(P * t, P)], start=True, stop=False)
                    if c == 0:
                        for e in range(2):
                            pe.wait_ge(z_moved[e], t + 1)
                    for g in range(GT):
                        last = nc.tensor.matmul(acc, w1_sb[:, g, n], z_sb[:, g, :], start=False, stop=(g == GT - 1))
                    if i == C1 // 2 - 1:
                        last.then_inc(h1_made[s], 1)

            def layer2(t):
                for m in range(C2):
                    for c in range(C1):
                        if m == 0 and c % (C1 // 2) == 0:
                            pe.wait_ge(h1_kept[c // (C1 // 2)], t + 1)
                        last = nc.tensor.matmul(h2_ps[:, P * m:P * m + P], w2_sb[:, c, P * m:P * m + P],
                                                h1_sb[:, c, :], start=(c == 0), stop=(c == C1 - 1))
                last.then_inc(h2_made, 1)

            def layer3(t):
                pe.wait_ge(h2_kept, t + 1)
                for m in range(C2):
                    last = nc.tensor.matmul(y_ps[:, 0:1], h2_sb[:, m, :], w3_sb[:, m:m + 1],
                                            start=(m == 0), stop=(m == C2 - 1))
                last.then_inc(y_made, 1)

            pe.wait_ge(ident_made, 1)
            for i in range(WARM):
                nc.tensor.transpose(tr_ps[0][:, i % TG, :], ident[:, :], ident[:, :])
            for i in range(NPF):
                pick(i)
                if i in AFTER_PICK:
                    transpose(0, AFTER_PICK[i], True)
            interact(0)

            def step(t, layer3_due):
                for k in range(len(GROUPS)):
                    transpose(t, k, False)
                    if k == 1 and layer3_due:
                        layer3(t - 2)
                    elif k == 1:
                        pe.wait_ge(w_loaded, 16 * N_W)
                        pe.wait_ge(pick_kept, NPF)
                    if k in L1_AFTER:
                        layer1(t - 1, L1_AFTER[k])
                interact(t)
                layer2(t - 1)

            step(1, False)
            with pe.Fori(2, NT) as t:
                step(t, True)
            layer1(NT - 1, (0,))
            layer3(NT - 2)
            layer1(NT - 1, (1, 2, 3))
            layer2(NT - 1)
            layer3(NT - 1)

        def copy_group(eng, copy, t, k):
            eng.wait_ge(transposed[k], t + 1)
            g = GROUPS[k]
            copy(vT[:, :, g[0]:g[-1] + 1].rearrange("d p f -> d f p"), tr_ps[k % 2][:, 0:len(g), :])\
                .then_inc(vt_copied[k], 1)

        def move_z(eng, s, copy, t):
            eng.wait_ge(z_made, t + 1)
            for j in (2 * s, 2 * s + 1):
                for r in range(SLOTS):
                    n = len(range(r, NZ, SLOTS))
                    src = z_ps[SLOT * j:SLOT * j + NZ, :, 0:QB * NZ]\
                        .rearrange("f h (q g) -> f g h q", g=NZ)[:, r:NZ:SLOTS]
                    dst = z_sb[SLOT * r:SLOT * r + NZ, 0:n, QN * j:QN * j + QN]\
                        .rearrange("f g (h q) -> f g h q", h=QH)
                    last = copy(dst, src)
            last.then_inc(z_moved[s], 1)

        @block.vector
        def _(dve):
            copy = nc.vector.tensor_copy

            def keep_h1(t):
                dve.wait_ge(h1_made[0], t + 1)
                for c in range(C1 // 2):
                    last = nc.vector.tensor_scalar(h1_sb[:, c, :], h1_ps[0][:, P * c:P * c + P], b1_sb[:, c:c + 1],
                                                   0.0, ALU.add, ALU.max)
                last.then_inc(h1_kept[0], 1)

            nc.vector.memset(ident[:, :], 0.0).then_inc(ident_zero, 1)
            nc.vector.memset(z_sb[:, :, :], 0.0).then_inc(z_cleared, 1)
            dve.wait_ge(row_id_made, 1)
            nc.vector.tensor_scalar(minus_row[:, :], row_id[:, R - 1:R], -1.0, None, ALU.mult).then_inc(minus_row_made, 1)
            for i in range(NPF):
                dve.wait_ge(picks_loaded[i], 16)
                if i >= 2:
                    dve.wait_ge(picked, i - 1)
                for r in range(R - 1):
                    nc.vector.tensor_scalar(hot[i % 2][:, r, :], picks[:, i, :], row_id[:, r:r + 1], None,
                                            ALU.is_equal).then_inc(hot_made, 1)
                dve.wait_ge(hi_made, i + 1)
                nc.vector.tensor_tensor(tbl_lo[:, i % 2, :, :], tbl[:, i, :, :], tbl_hi[:, i % 2, :, :].bitcast(F32),
                                        ALU.subtract).then_inc(lo_made, 1)
            dve.wait_ge(z_cleared, 1)
            move_z(dve, 0, copy, 0)
            dve.wait_ge(w_loaded, 16 * N_W)

            def step(t):
                for k in range(0, len(GROUPS), 2):
                    copy_group(dve, copy, t, k)
                    if k == 0:
                        keep_h1(t - 1)
                move_z(dve, 0, copy, t)

            step(1)
            with dve.Fori(2, NT) as t:
                step(t)
            keep_h1(NT - 1)

        @block.scalar
        def _(act):
            def copy(dst, src):
                return nc.scalar.activation(dst, src, ACT.Copy)

            def place_px(t):
                copy(vT[:, :, NGF:NV].rearrange("d p f -> d f p"), px[:, :, bass.ds(P * t, P)]).then_inc(px_placed, 1)

            def keep_h1(t):
                act.wait_ge(h1_made[1], t + 1)
                for i in range(C1 // 2):
                    c = C1 // 2 + i
                    last = nc.scalar.activation(h1_sb[:, c, :], h1_ps[1][:, P * i:P * i + P], ACT.Relu,
                                                bias=b1_sb[:, c:c + 1])
                last.then_inc(h1_kept[1], 1)

            def keep_h2(t):
                act.wait_ge(h2_made, t + 1)
                for m in range(C2):
                    last = nc.scalar.activation(h2_sb[:, m, :], h2_ps[:, P * m:P * m + P], ACT.Relu,
                                                bias=b2_sb[:, m:m + 1])
                last.then_inc(h2_kept, 1)

            def keep_y(t):
                act.wait_ge(y_made, t + 1)
                copy(y_sb[:, bass.ds(t, 1)], y_ps[:, 0:1]).then_inc(y_kept, 1)

            def keep_pick(i):
                act.wait_ge(picked, i + 1)
                first = copy(vT[:, :, NGF + i], h1_ps[i % 2][:, 0:P])
                if i == NPF - 1:
                    first.then_inc(px_placed, 1)
                copy(px[:, i, :], h1_ps[i % 2][:, 0:B]).then_inc(pick_kept, 1)

            def last_hot(i):
                act.wait_ge(picks_loaded[i], 16)
                act.wait_ge(minus_row_made, 1)
                nc.scalar.activation(apart[:, i % 2, :], picks[:, i, :], ACT.Abs, bias=minus_row[:, :]).then_inc(apart_made, 1)
                act.wait_ge(apart_made, i + 1)
                nc.scalar.activation(hot[i % 2][:, R - 1, :], apart[:, i % 2, :], ACT.Relu, bias=1.0, scale=-1.0)\
                    .then_inc(last_hot_made, 1)

            for i in range(NPF):
                act.wait_ge(tbl_loaded[i], 16)
                if i >= 2:
                    act.wait_ge(picked, i - 1)
                copy(tbl_hi[:, i % 2, :, :], tbl[:, i, :, :]).then_inc(hi_made, 1)
                last_hot(i)
                if i >= 2:
                    keep_pick(i - 2)
                    if i - 2 in AFTER_PICK:
                        copy_group(act, copy, 0, AFTER_PICK[i - 2])
            act.wait_ge(x_loaded, 16)
            copy(vT[:, :, NF], px[:, NPF, 0:P])
            for i in (NPF - 2, NPF - 1):
                keep_pick(i)
                if i in AFTER_PICK:
                    copy_group(act, copy, 0, AFTER_PICK[i])
            act.wait_ge(pick_kept, NPF)
            act.wait_ge(z_cleared, 1)
            move_z(act, 1, copy, 0)
            act.wait_ge(w_loaded, 16 * N_W)

            def step(t, layer3_due):
                place_px(t)
                for k in range(1, len(GROUPS), 2):
                    copy_group(act, copy, t, k)
                    if k == 1 and layer3_due:
                        keep_y(t - 2)
                keep_h1(t - 1)
                move_z(act, 1, copy, t)
                keep_h2(t - 1)

            step(1, False)
            with act.Fori(2, NT) as t:
                step(t, True)
            keep_y(NT - 2)
            keep_h1(NT - 1)
            keep_h2(NT - 1)
            keep_y(NT - 1)


def kernel(**inputs):
    import numpy as np
    import concourse.bacc as bacc
    from concourse.bass_utils import run_bass_kernel_spmd

    nc = bacc.Bacc("TRN2", target_bir_lowering=False, num_devices=1)
    arrays = {}

    def dram(name, a):
        arrays[name] = np.ascontiguousarray(a)
        return nc.dram_tensor(name, a.shape, mybir.dt.from_np(a.dtype), kind="ExternalInput").ap()

    x = np.asarray(inputs["r_dense_x"])
    ids = np.asarray(inputs["ids"])
    tables = [np.asarray(inputs[f"tbl_{i}"]) for i in range(NF)]
    W1 = np.asarray(inputs["W_top1"])
    NT = x.shape[0] // P
    gathered, picked = feature_order([a.shape[0] for a in tables])
    order = gathered + picked + [NF]
    pair = {fg: n for n, fg in enumerate(zip(*(i.tolist() for i in np.triu_indices(NV, k=1))))}
    w1 = np.zeros((P, GT, W1.shape[1]), W1.dtype)
    for b in range(1, NV):
        for a in range(b):
            w1[SLOT * ((b - 1) % SLOTS) + a, (b - 1) // SLOTS] = W1[pair[min(order[a], order[b]), max(order[a], order[b])]]

    def by_tile(a):
        return a.reshape(a.shape[0], P, NT).transpose(0, 2, 1).reshape(a.shape)

    args = [dram("xT", by_tile(x.T)), dram("ids", ids), dram("ids_rows", by_tile(ids.T[picked])),
            [dram(f"tbl_{i}", a) for i, a in enumerate(tables)],
            dram("w1", w1), dram("w1x", W1[len(pair):]),
            dram("b1", np.asarray(inputs["b_top1"]).reshape(-1, P).T),
            dram("w2", np.asarray(inputs["W_top2"])),
            dram("b2", np.asarray(inputs["b_top2"]).reshape(-1, P).T),
            dram("w3", np.asarray(inputs["W_top3"]).reshape(-1, P).T)]
    out = nc.dram_tensor("y", (x.shape[0], 1), F32, kind="ExternalOutput").ap()
    dlrm_tower(nc, *args, out)
    return run_bass_kernel_spmd(nc, [arrays], core_ids=[0]).results[0]["y"]
```

```python
import concourse.bass as bass
from concourse import mybir
from contextlib import ExitStack

ALU = mybir.AluOpType
ACT = mybir.ActivationFunctionType
F32 = mybir.dt.float32
F32R = mybir.dt.float32r
I32 = mybir.dt.int32
U32 = mybir.dt.uint32

P = 128
BANK = 512
NF = 26
NV = NF + 1
HALF = NV // 2
SLOT = 32
SLOTS = P // SLOT
SHARED = SLOTS - 1
GT = (HALF - 1) // SHARED
ALONE = NV - 2 * SHARED * GT
TG = 4
QB = 16
WARM = 23
EARLY = 8
LATE = 1


def feature_order(n_rows):
    by_size = sorted(range(NF), key=lambda f: n_rows[f])
    early, late = by_size[:EARLY], by_size[EARLY:EARLY + LATE]
    gathered = [f for f in range(NF) if f not in early + late]
    return gathered, late, early


def lower_column(r, g):
    return 1 + SHARED * g + r if r < SHARED else HALF * g


def has_upper(r, c, a):
    return r < SHARED and (a < c or a > c + HALF)


def dlrm_tower(nc, xT, ids, ids_rows, tables, upper, w1, w1x, b1, w2, b2, w3, out):
    B = ids.shape[0]
    D = xT.shape[0]
    N1, N2 = w2.shape
    C1, C2 = N1 // P, N2 // P
    NT = B // P
    QN = P // SLOTS
    QH = QN // QB
    gathered_f, late_f, early_f = feature_order([a.shape[0] for a in tables])
    GF = gathered_f + late_f
    PF = early_f + late_f
    NPF = len(PF)
    NG = len(gathered_f)
    entry = [LATE + i for i in range(EARLY)] + list(range(LATE))
    DENSE = NPF

    def groups(n):
        return [range(a, min(a + TG, n)) for a in range(0, n, TG)]

    GROUPS_0, GROUPS = groups(NG + LATE), groups(NG)
    LAST = len(GROUPS) - 1
    AFTER_PICK = {EARLY - 1 - len(GROUPS_0) + k: k for k in range(len(GROUPS_0))}
    ALL = (GT, *range(GT))
    CUT = 2
    L1_AFTER = {1: ((0, ALL),), 2: ((1, ALL), (2, ALL)), LAST - 1: ((3, ALL[:CUT]),), LAST: ((3, ALL[CUT:]),)}
    assert LAST - 1 > 2 and ALONE <= GT
    assert C1 == 4 and C2 == 2
    W_AFTER = EARLY - 1
    AHEAD = 4
    KP = max(p for p in range(1, P + 1) if all(tables[f].shape[0] % p == 0 for f in PF))
    PLACES = [tables[f].shape[0] // KP for f in PF]
    R_MAX = max(PLACES)
    assert len(set(PLACES[:EARLY])) == 1 and len(set(PLACES[EARLY:])) <= 1
    HOTS = [sum(r - 1 for r in PLACES[:i]) for i in range(NPF)]
    assert D == P and QB * NV <= BANK and B <= BANK

    ctx = ExitStack()
    with ctx:
        def sb(name, shape, dt=F32):
            return ctx.enter_context(nc.sbuf_tensor(name, shape, dt))

        def pb(name, shape):
            return ctx.enter_context(nc.psum_tensor(name, shape, F32))

        def sem(name):
            return ctx.enter_context(nc.semaphore(name))

        ident = sb("ident", [P, P])
        row_id = [sb(f"row_id{s}", [KP, R_MAX], I32) for s in range(2)]
        minus_row = [sb(f"minus_row{s}", [KP, 1]) for s in range(2)]
        apart = sb("apart", [KP, 2, B])
        idx = sb("idx", [P, NT, NF], I32)
        picks = sb("picks", [KP, NPF, B], I32)
        tbl = sb("tbl", [KP, AHEAD, R_MAX, D])
        tbl_hi = sb("tbl_hi", [KP, 2, R_MAX, D], F32R)
        tbl_lo = sb("tbl_lo", [KP, 2, R_MAX, D], F32R)
        hot = [sb(f"hot{i}", [KP, R_MAX, B], F32R) for i in range(2)]
        px = sb("px", [D, NPF + 1, B])
        w1_sb = sb("w1_sb", [P, GT, N1])
        w1x_sb = sb("w1x_sb", [D, N1])
        w2_sb = sb("w2_sb", [P, C1, N2])
        w3_sb = sb("w3_sb", [P, C2])
        b1_sb = sb("b1_sb", [P, C1])
        b2_sb = sb("b2_sb", [P, C2])
        rows = sb("rows", [P, NG + LATE, D])
        upper_sb = sb("upper_sb", [P, GT], I32)
        vT = sb("vT", [D, P, NV])
        z_sb = sb("z_sb", [P, GT, P])
        h1_sb = sb("h1_sb", [P, C1, P])
        h2_sb = sb("h2_sb", [P, 2, C2, P])
        y_sb = sb("y_sb", [P, NT])

        tr_ps = [pb(f"tr_ps{i}", [P, TG, P]) for i in range(2)]
        z_ps = pb("z_ps", [P, QH, BANK])
        h1_ps = [pb(f"h1_ps{s}", [P, BANK]) for s in range(2)]
        h2_ps = [pb(f"h2_ps{m}", [P, BANK]) for m in range(C2)]
        y_ps = z_ps[:, 0, QB * NV:QB * NV + NT]

        ids_loaded = sem("ids_loaded")
        picks_loaded = [sem(f"picks_loaded{i}") for i in range(NPF)]
        tbl_loaded = [sem(f"tbl_loaded{i}") for i in range(NPF)]
        w_loaded = sem("w_loaded")
        x_loaded = sem("x_loaded")
        ident_zero = sem("ident_zero")
        ident_made = sem("ident_made")
        row_id_made = sem("row_id_made")
        z_cleared = sem("z_cleared")
        hi_made = sem("hi_made")
        lo_made = sem("lo_made")
        minus_row_made = sem("minus_row_made")
        hot_made = sem("hot_made")
        apart_made = sem("apart_made")
        last_hot_made = sem("last_hot_made")
        picked = sem("picked")
        pick_kept = sem("pick_kept")
        gathered = [sem(f"gathered{k}") for k in range(len(GROUPS_0))]
        transposed = [sem(f"transposed{k}") for k in range(len(GROUPS_0))]
        vt_copied = [sem(f"vt_copied{k}") for k in range(len(GROUPS_0))]
        px_placed = sem("px_placed")
        z_made = [sem(f"z_made{h}") for h in range(QH)]
        lower_moved = [[sem(f"lower_moved{h}_{j}") for j in range(SLOTS)] for h in range(QH)]
        z_moved = sem("z_moved")
        h1_made = [sem(f"h1_made{c}") for c in range(C1)]
        h1_kept = [sem(f"h1_kept{c}") for c in range(C1)]
        h2_made = [sem(f"h2_made{m}") for m in range(C2)]
        h2_kept = [sem(f"h2_kept{m}") for m in range(C2)]
        y_made = sem("y_made")
        y_kept = sem("y_kept")
        stored = sem("stored")
        N_W = 7

        block = ctx.enter_context(nc.Block())

        def pick_cols(i):
            return slice(0 if i < EARLY else P, B)

        @block.sync
        def _(sp):
            sp.dma_start(idx[:, :, :], ids.rearrange("(p t) f -> p t f", t=NT)).then_inc(ids_loaded, 16)
            for i, f in enumerate(PF):
                sp.dma_start(picks[:, i, :], ids_rows[i:i + 1, :].broadcast_to([KP, B])).then_inc(picks_loaded[i], 16)
                if i >= AHEAD:
                    sp.wait_ge(hi_made, i - AHEAD + 1)
                    sp.wait_ge(lo_made, i - AHEAD + 1)
                sp.dma_start(tbl[:, i % AHEAD, 0:PLACES[i], :], tables[f].rearrange("(p r) d -> p r d", p=KP))\
                    .then_inc(tbl_loaded[i], 16)
            sp.dma_start(px[:, DENSE, :], xT).then_inc(x_loaded, 16)
            sp.wait_ge(hi_made, W_AFTER)
            for dst, src in ((upper_sb, upper), (b1_sb, b1), (b2_sb, b2), (w3_sb, w3), (w1x_sb, w1x), (w1_sb, w1),
                             (w2_sb, w2.rearrange("(c p) n -> p c n", p=P))):
                sp.dma_start(dst[:], src).then_inc(w_loaded, 16)
            sp.wait_ge(y_kept, 1)
            sp.dma_start(out.rearrange("(p t) o -> p (t o)", t=NT), y_sb[:, :]).then_inc(stored, 16)
            sp.wait_ge(stored, 16)

        @block.gpsimd
        def _(pool):
            for s in range(2):
                pool.iota(row_id[s][:, :], [[1, R_MAX]], base=0, channel_multiplier=PLACES[-s]).then_inc(row_id_made, 1)
            pool.wait_ge(ident_zero, 1)
            pool.affine_select(out=ident[:, :], in_=ident[:, :], compare_op=ALU.not_equal, fill=1.0,
                               base=0, pattern=[[-1, P]], channel_multiplier=1).then_inc(ident_made, 1)
            pool.wait_ge(ids_loaded, 16)
            for t in range(NT):
                for k, group in enumerate(GROUPS if t else GROUPS_0):
                    if t:
                        pool.wait_ge(transposed[k], t)
                    for u in group:
                        pool.indirect_dma_start(
                            rows[:, u, :], None, tables[GF[u]],
                            bass.IndirectOffsetOnAxis(idx[:, t, GF[u]:GF[u] + 1].bitcast(U32), 0),
                        ).then_inc(gathered[k], 16)

        @block.tensor
        def _(pe):
            def pick(i):
                R, cols = PLACES[i], pick_cols(i)
                acc = h1_ps[i % 2][:, cols]
                if i >= 2:
                    pe.wait_ge(pick_kept, i - 1)
                pe.wait_ge(hi_made, i + 1)
                for r in range(R):
                    if r < R - 1:
                        pe.wait_ge(hot_made, HOTS[i] + r + 1)
                    else:
                        pe.wait_ge(last_hot_made, i + 1)
                    nc.tensor.matmul(acc, tbl_hi[:, i % 2, r, :], hot[i % 2][:, r, cols], start=(r == 0), stop=False)
                pe.wait_ge(lo_made, i + 1)
                for r in range(R):
                    last = nc.tensor.matmul(acc, tbl_lo[:, i % 2, r, :], hot[i % 2][:, r, cols],
                                            start=False, stop=(r == R - 1))
                last.then_inc(picked, 1)

            def transpose(t, k, of_tile, before):
                pe.wait_ge(gathered[k], 16 * (len(GROUPS_0[k]) + t * len(GROUPS[k])) if before else 16 * len(of_tile[k]))
                if k >= 2:
                    pe.wait_ge(vt_copied[k - 2], t + 1)
                elif before:
                    pe.wait_ge(vt_copied[max(j for j in range(len(before)) if j % 2 == k)], t)
                for i, u in enumerate(of_tile[k]):
                    last = nc.tensor.transpose(tr_ps[k % 2][:, i, :], rows[:, u, :], ident[:, :])
                last.then_inc(transposed[k], 1)

            def interact(t, of_tile):
                for k in range(len(of_tile)):
                    pe.wait_ge(vt_copied[k], t + 1)
                pe.wait_ge(px_placed, t + 1)
                for q in range(QN):
                    for j in range(SLOTS):
                        v = vT[:, QN * j + q, :]
                        c = NV * (q % QB)
                        last = nc.tensor.matmul(z_ps[SLOT * j:SLOT * j + NV, q // QB, c:c + NV], v, v,
                                                start=True, stop=True)
                    if q % QB == QB - 1:
                        last.then_inc(z_made[q // QB], 1)

            def layer1(t, c, k_tiles):
                n = slice(P * c, P * c + P)
                acc = h1_ps[c % 2][:, P * (c // 2):P * (c // 2) + P]
                for g in k_tiles:
                    if g == GT:
                        if c >= 2:
                            pe.wait_ge(h1_kept[c - 2], t + 1)
                        w, z = w1x_sb[:, n], px[:, DENSE, bass.ds(P * t, P)]
                    else:
                        if c == 0 and g == 0:
                            pe.wait_ge(z_moved, t + 1)
                        w, z = w1_sb[:, g, n], z_sb[:, g, :]
                    last = nc.tensor.matmul(acc, w, z, start=(g == GT), stop=(g == GT - 1))
                if k_tiles[-1] == GT - 1:
                    last.then_inc(h1_made[c], 1)

            def layer2(t):
                for m in range(C2):
                    for c in range(C1):
                        if m == 0:
                            pe.wait_ge(h1_kept[c], t + 1)
                        last = nc.tensor.matmul(h2_ps[m][:, 0:P], w2_sb[:, c, P * m:P * m + P],
                                                h1_sb[:, c, :], start=(c == 0), stop=(c == C1 - 1))
                    last.then_inc(h2_made[m], 1)

            def layer3(t, s=0):
                for m in range(C2):
                    pe.wait_ge(h2_kept[m], t + 1)
                    last = nc.tensor.matmul(y_ps[:, bass.ds(t, 1)], h2_sb[:, s, m, :], w3_sb[:, m:m + 1],
                                            start=(m == 0), stop=(m == C2 - 1))
                last.then_inc(y_made, 1)

            pe.wait_ge(ident_made, 1)
            for i in range(WARM):
                nc.tensor.transpose(tr_ps[0][:, i % TG, :], ident[:, :], ident[:, :])
            for i in range(EARLY):
                pick(i)
                if i in AFTER_PICK:
                    transpose(0, AFTER_PICK[i], GROUPS_0, None)
            for k in range(2):
                transpose(1, k, GROUPS, GROUPS_0)
            interact(0, GROUPS_0)
            for i in range(EARLY, NPF):
                pick(i)
            transpose(1, 2, GROUPS, GROUPS_0)
            TRANSPOSED = 3
            pe.wait_ge(w_loaded, 16 * N_W)
            pe.wait_ge(pick_kept, NPF)

            def step(t, first):
                for k in range(len(GROUPS)):
                    if not (first and k < TRANSPOSED):
                        transpose(t, k, GROUPS, GROUPS_0 if first else GROUPS)
                    for c, k_tiles in L1_AFTER.get(k, ()):
                        layer1(t - 1, c, k_tiles)
                    if k == 1 and not first:
                        layer3(t - 2)
                interact(t, GROUPS)
                layer2(t - 1)

            step(1, True)
            with pe.Fori(2, NT) as t:
                step(t, False)
            for c in range(C1):
                layer1(NT - 1, c, ALL)
            layer2(NT - 1)
            layer3(NT - 2)
            layer3(NT - 1, 1)

        def copy_group(eng, copy, t, k, of_tile):
            eng.wait_ge(transposed[k], t + 1)
            g = of_tile[k]
            copy(vT[:, :, g[0]:g[-1] + 1].rearrange("d p f -> d f p"), tr_ps[k % 2][:, 0:len(g), :])\
                .then_inc(vt_copied[k], 1)

        def z_part(h, j, r, upper):
            n = GT if r < SHARED else ALONE
            c = lower_column(r, 0) + upper * HALF
            stride = lower_column(r, 1) - lower_column(r, 0)
            src = z_ps[SLOT * j:SLOT * j + NV, h, 0:QB * NV]\
                .rearrange("f (q g) -> f g q", g=NV)[:, c:c + stride * (n - 1) + 1:stride]
            at = QN * j + QB * h
            dst = z_sb[SLOT * r:SLOT * r + NV, 0:n, at:at + QB]
            return dst, src

        @block.vector
        def _(dve):
            copy = nc.vector.tensor_copy

            def keep_h1(t, c):
                dve.wait_ge(h1_made[c], t + 1)
                nc.vector.tensor_scalar(h1_sb[:, c, :], h1_ps[0][:, P * (c // 2):P * (c // 2) + P], b1_sb[:, c:c + 1],
                                        0.0, ALU.add, ALU.max).then_inc(h1_kept[c], 1)

            def place_upper(t):
                for h in range(QH):
                    for j in range(SLOTS):
                        dve.wait_ge(w_loaded, 16 * N_W)
                        dve.wait_ge(lower_moved[h][j], t + 1)
                        for r in range(SHARED):
                            dst, src = z_part(h, j, r, True)
                            mask = upper_sb[SLOT * r:SLOT * r + NV, :].unsqueeze(2).broadcast_to([NV, GT, QB])
                            last = nc.vector.copy_predicated(dst, mask, src)
                last.then_inc(z_moved, 1)

            nc.vector.memset(ident[:, :], 0.0).then_inc(ident_zero, 1)
            nc.vector.memset(z_sb[:, :, :], 0.0).then_inc(z_cleared, 1)
            dve.wait_ge(row_id_made, 2)
            for s in range(2):
                R = PLACES[-s]
                nc.vector.tensor_scalar(minus_row[s][:, :], row_id[s][:, R - 1:R], -1.0, None, ALU.mult)\
                    .then_inc(minus_row_made, 1)
            for i in range(NPF):
                R, cols = PLACES[i], pick_cols(i)
                dve.wait_ge(picks_loaded[i], 16)
                if i >= 2:
                    dve.wait_ge(picked, i - 1)
                for r in range(R - 1):
                    nc.vector.tensor_scalar(hot[i % 2][:, r, cols], picks[:, i, cols], row_id[i >= EARLY][:, r:r + 1], None,
                                            ALU.is_equal).then_inc(hot_made, 1)
                dve.wait_ge(hi_made, i + 1)
                nc.vector.tensor_tensor(tbl_lo[:, i % 2, 0:R, :], tbl[:, i % AHEAD, 0:R, :], tbl_hi[:, i % 2, 0:R, :].bitcast(F32),
                                        ALU.subtract).then_inc(lo_made, 1)
            dve.wait_ge(z_made[QH - 1], 1)
            copy_group(dve, copy, 1, 0, GROUPS)
            place_upper(0)

            def step(t, first):
                if not first:
                    copy_group(dve, copy, t, 0, GROUPS)
                keep_h1(t - 1, 0)
                copy_group(dve, copy, t, 2, GROUPS)
                keep_h1(t - 1, 2)
                for k in range(4, len(GROUPS), 2):
                    copy_group(dve, copy, t, k, GROUPS)
                place_upper(t)

            step(1, True)
            with dve.Fori(2, NT) as t:
                step(t, False)
            for c in (0, 2):
                keep_h1(NT - 1, c)

        @block.scalar
        def _(act):
            def copy(dst, src):
                return nc.scalar.activation(dst, src, ACT.Copy)

            def place_px(t):
                copy(vT[:, :, NG:NV].rearrange("d p f -> d f p"), px[:, :, bass.ds(P * t, P)]).then_inc(px_placed, 1)

            def move_lower(t):
                for h in range(QH):
                    act.wait_ge(z_made[h], t + 1)
                    for j in range(SLOTS):
                        for r in range(SLOTS):
                            dst, src = z_part(h, j, r, False)
                            last = copy(dst, src)
                        last.then_inc(lower_moved[h][j], 1)

            def keep_h1(t, c):
                act.wait_ge(h1_made[c], t + 1)
                nc.scalar.activation(h1_sb[:, c, :], h1_ps[1][:, P * (c // 2):P * (c // 2) + P], ACT.Relu,
                                     bias=b1_sb[:, c:c + 1]).then_inc(h1_kept[c], 1)

            def keep_h2(t, s=0):
                for m in range(C2):
                    act.wait_ge(h2_made[m], t + 1)
                    nc.scalar.activation(h2_sb[:, s, m, :], h2_ps[m][:, 0:P], ACT.Relu,
                                         bias=b2_sb[:, m:m + 1]).then_inc(h2_kept[m], 1)

            def keep_pick(i):
                act.wait_ge(picked, i + 1)
                if i < EARLY:
                    first = copy(vT[:, :, NG + entry[i]], h1_ps[i % 2][:, 0:P])
                    if i == EARLY - 1:
                        first.then_inc(px_placed, 1)
                copy(px[:, entry[i], pick_cols(i)], h1_ps[i % 2][:, pick_cols(i)]).then_inc(pick_kept, 1)
                if i in AFTER_PICK:
                    copy_group(act, copy, 0, AFTER_PICK[i], GROUPS_0)

            def prepare_pick(i):
                R, cols, s = PLACES[i], pick_cols(i), int(i >= EARLY)
                act.wait_ge(tbl_loaded[i], 16)
                if i >= 2:
                    act.wait_ge(picked, i - 1)
                copy(tbl_hi[:, i % 2, 0:R, :], tbl[:, i % AHEAD, 0:R, :]).then_inc(hi_made, 1)
                act.wait_ge(picks_loaded[i], 16)
                act.wait_ge(minus_row_made, s + 1)
                nc.scalar.activation(apart[:, i % 2, cols], picks[:, i, cols], ACT.Abs, bias=minus_row[s][:, :])\
                    .then_inc(apart_made, 1)
                act.wait_ge(apart_made, i + 1)
                nc.scalar.activation(hot[i % 2][:, R - 1, cols], apart[:, i % 2, cols], ACT.Relu, bias=1.0, scale=-1.0)\
                    .then_inc(last_hot_made, 1)

            for i in range(EARLY):
                prepare_pick(i)
                if i >= 2:
                    keep_pick(i - 2)
            act.wait_ge(x_loaded, 16)
            copy(vT[:, :, NF], px[:, DENSE, 0:P])
            for i in range(EARLY, NPF):
                keep_pick(i - 2)
                prepare_pick(i)
            for i in range(NPF - 2, EARLY):
                keep_pick(i)
            act.wait_ge(z_cleared, 1)
            move_lower(0)
            for i in range(max(NPF - 2, EARLY), NPF):
                keep_pick(i)
            act.wait_ge(pick_kept, NPF)
            act.wait_ge(w_loaded, 16 * N_W)

            def step(t):
                copy_group(act, copy, t, 1, GROUPS)
                place_px(t)
                keep_h1(t - 1, 1)
                copy_group(act, copy, t, 3, GROUPS)
                keep_h1(t - 1, 3)
                move_lower(t)
                keep_h2(t - 1)

            step(1)
            with act.Fori(2, NT) as t:
                step(t)
            for c in (1, 3):
                keep_h1(NT - 1, c)
            keep_h2(NT - 1, 1)
            act.wait_ge(y_made, NT)
            copy(y_sb[:, :], y_ps).then_inc(y_kept, 1)


def kernel(**inputs):
    import numpy as np
    import concourse.bacc as bacc
    from concourse.bass_utils import run_bass_kernel_spmd

    nc = bacc.Bacc("TRN2", target_bir_lowering=False, num_devices=1)
    arrays = {}

    def dram(name, a):
        arrays[name] = np.ascontiguousarray(a)
        return nc.dram_tensor(name, a.shape, mybir.dt.from_np(a.dtype), kind="ExternalInput").ap()

    x = np.asarray(inputs["r_dense_x"])
    ids = np.asarray(inputs["ids"])
    tables = [np.asarray(inputs[f"tbl_{i}"]) for i in range(NF)]
    W1 = np.asarray(inputs["W_top1"])
    NT = x.shape[0] // P
    gathered, late, early = feature_order([a.shape[0] for a in tables])
    order = gathered + late + early + [NF]
    pair = {fg: n for n, fg in enumerate(zip(*(i.tolist() for i in np.triu_indices(NV, k=1))))}
    w1 = np.zeros((P, GT, W1.shape[1]), W1.dtype)
    upper = np.zeros((P, GT), np.int32)
    left = dict(pair)
    for g in range(GT):
        for r in range(SLOTS if g < ALONE else SHARED):
            for a in range(NV):
                c = lower_column(r, g)
                at = SLOT * r + a, g
                upper[at] = has_upper(r, c, a)
                c += HALF * upper[at]
                n = left.pop((min(order[a], order[c]), max(order[a], order[c])), None)
                if n is not None:
                    w1[at] = W1[n]
    assert not left

    def by_tile(a):
        return a.reshape(a.shape[0], P, NT).transpose(0, 2, 1).reshape(a.shape)

    args = [dram("xT", by_tile(x.T)), dram("ids", ids), dram("ids_rows", by_tile(ids.T[early + late])),
            [dram(f"tbl_{i}", a) for i, a in enumerate(tables)],
            dram("upper", upper), dram("w1", w1), dram("w1x", W1[len(pair):]),
            dram("b1", np.asarray(inputs["b_top1"]).reshape(-1, P).T),
            dram("w2", np.asarray(inputs["W_top2"])),
            dram("b2", np.asarray(inputs["b_top2"]).reshape(-1, P).T),
            dram("w3", np.asarray(inputs["W_top3"]).reshape(-1, P).T)]
    out = nc.dram_tensor("y", (x.shape[0], 1), F32, kind="ExternalOutput").ap()
    dlrm_tower(nc, *args, out)
    return run_bass_kernel_spmd(nc, [arrays], core_ids=[0]).results[0]["y"]
```
